# Optimizing a Trainium2 kernel written in Bass

```python
import numpy as np
import jax
import jax.numpy as jnp

def _softmax(x, axis=-1):
    return jax.nn.softmax(x, axis=axis)

def _gelu(x):
    return jax.nn.gelu(x, approximate=True)

def _silu(x):
    return jax.nn.silu(x)

def _sigmoid(x):
    return jax.nn.sigmoid(x)

def _layernorm(x, axis=-1, eps=1e-05):
    m = jnp.mean(x, axis=axis, keepdims=True)
    v = jnp.var(x, axis=axis, keepdims=True)
    return (x - m) / jnp.sqrt(v + eps)

def _scatter_add(tgt, idx, src, axis=0):
    return tgt.at[idx].add(src)

def _segment_sum(src, seg, n):
    return jax.ops.segment_sum(src, seg, n)
kernel_name = 'mk_early_fusion_d1_tok_img768_r4_d576d0'

def setup_inputs(seed: int=0):
    np.random.seed(seed)
    _w = jnp.asarray

    def _rec_inputs():
        import jax
        import jax.numpy as jnp
        _rk = jax.random.key(seed)
        x = -0.000147625 + 0.999875 * jax.random.normal(jax.random.fold_in(_rk, 1), (32, 12, 224, 224), jnp.float32)
        txt = -0.0221329 + 10 * jax.random.normal(jax.random.fold_in(_rk, 2), (32, 77, 192), jnp.float32)
        return (x, txt)
    x, txt = _rec_inputs()

    def _L0_tok_setup():
        import jax, jax.numpy as jnp
        import numpy as np
        IMG = 224
        PATCH = 16
        EMBED = 192
        C = 12
        B = 64
        key = jax.random.key(seed)
        k1, k2 = jax.random.split(key)
        x = jax.random.normal(k1, (B, C, IMG, IMG), dtype=jnp.float32)
        channel_weights = jax.random.normal(k2, (C, EMBED), dtype=jnp.float32)
        return {'x': x, 'channel_weights': channel_weights}
    _L0_tok_all = _L0_tok_setup()
    _L0_tok_in = {k: v for k, v in _L0_tok_all.items() if k in ('channel_weights',)}
    del _L0_tok_all

    def _L0_attn_setup():
        import jax, jax.numpy as jnp
        import numpy as np
        D_MODEL = 192
        EXPAND = 4
        D_INNER = EXPAND * D_MODEL
        D_HEAD = 64
        N_HEADS = D_INNER // D_HEAD
        N_EXPERTS = 8
        TOP_K = 2
        R3 = 64
        R2 = 256
        EPS = 1e-05
        TANH_SCALE = 10.0
        ROUTER_TEMP = 0.5

        def _rms_norm(x, w):
            return x * jax.lax.rsqrt(jnp.mean(x * x, axis=-1, keepdims=True) + EPS) * w

        def _scaled_tanh(x):
            return TANH_SCALE * jnp.tanh(x * (1.0 / TANH_SCALE))
        key = jax.random.key(seed)
        ks = jax.random.split(key, 13)
        s = 0.02
        B, L = (2, 1024)
        return {'x': jax.random.normal(ks[0], (B, L, D_MODEL), dtype=jnp.float32), 'rms1_w': jnp.ones((D_MODEL,), jnp.float32), 'W_in': s * jax.random.normal(ks[1], (D_MODEL, 2 * D_INNER + N_HEADS), jnp.float32), 'dt_bias': jax.random.uniform(ks[2], (N_HEADS,), jnp.float32, -4.0, -1.0), 'W_out': s * jax.random.normal(ks[3], (D_INNER, D_MODEL), jnp.float32), 'ls1': 0.01 * jnp.ones((D_MODEL,), jnp.float32), 'rms2_w': jnp.ones((D_MODEL,), jnp.float32), 'W_down': s * jax.random.normal(ks[4], (D_MODEL, R3), jnp.float32), 'W_router': s * jax.random.normal(ks[5], (D_MODEL, N_EXPERTS), jnp.float32), 'G': s * jax.random.normal(ks[6], (N_EXPERTS, R3, R2), jnp.float32), 'W_up': s * jax.random.normal(ks[7], (R2, D_MODEL), jnp.float32), 'ls2': 0.01 * jnp.ones((D_MODEL,), jnp.float32)}
    _L0_attn_all = _L0_attn_setup()
    _L0_attn_in = {k: v for k, v in _L0_attn_all.items() if k in ('rms1_w', 'W_in', 'dt_bias', 'W_out', 'ls1', 'rms2_w', 'W_down', 'W_router', 'G', 'W_up', 'ls2')}
    del _L0_attn_all

    def _L0_ffn_setup():
        import jax, jax.numpy as jnp
        import numpy as np
        from jax import lax
        B, N, C, H = (64, 197, 192, 768)

        def quantize_linear(x, W, b):
            sf = lax.stop_gradient(jnp.mean(jnp.abs(W), axis=1, keepdims=True))
            rw = W - jnp.mean(W, axis=-1, keepdims=True)
            bw = sf * jnp.sign(rw)
            cw = jnp.clip(rw, -1.0, 1.0)
            weight = lax.stop_gradient(bw) - lax.stop_gradient(cw) + cw
            ci = jnp.clip(x, -1.0, 1.0)
            ba = lax.stop_gradient(jnp.sign(x)) - lax.stop_gradient(ci) + ci
            return jnp.einsum('bnc,hc->bnh', ba, weight) + b
        key = jax.random.key(seed)
        ks = jax.random.split(key, 4)
        x = jax.random.normal(ks[0], (B, N, C), dtype=jnp.float32)
        w1 = jax.random.normal(ks[1], (H, C), dtype=jnp.float32) * 0.02
        b1 = jnp.zeros((H,), dtype=jnp.float32)
        w2 = jax.random.normal(ks[2], (C, H), dtype=jnp.float32) * 0.02
        b2 = jnp.zeros((C,), dtype=jnp.float32)
        mfc1 = jnp.zeros((1, 1, 1), dtype=jnp.float32)
        mact1 = jnp.zeros((1, 1, 1), dtype=jnp.float32)
        mact2 = jnp.zeros((1, 1, 1), dtype=jnp.float32)
        mfc2 = jnp.zeros((1, 1, 1), dtype=jnp.float32)
        prelu_a = jnp.full((1,), 0.25, dtype=jnp.float32)
        return {'x': x, 'w1': w1, 'b1': b1, 'w2': w2, 'b2': b2, 'mfc1': mfc1, 'mact1': mact1, 'mact2': mact2, 'mfc2': mfc2, 'prelu_a': prelu_a}
    _L0_ffn_all = _L0_ffn_setup()
    _L0_ffn_in = {k: v for k, v in _L0_ffn_all.items() if k in ('w1', 'b1', 'w2', 'b2', 'mfc1', 'mact1', 'mact2', 'mfc2', 'prelu_a')}
    del _L0_ffn_all
    return {'x': x, 'txt': txt, 'L0_tok_channel_weights': _L0_tok_in['channel_weights'], 'L0_attn_rms1_w': _L0_attn_in['rms1_w'], 'L0_attn_W_in': _L0_attn_in['W_in'], 'L0_attn_dt_bias': _L0_attn_in['dt_bias'], 'L0_attn_W_out': _L0_attn_in['W_out'], 'L0_attn_ls1': _L0_attn_in['ls1'], 'L0_attn_rms2_w': _L0_attn_in['rms2_w'], 'L0_attn_W_down': _L0_attn_in['W_down'], 'L0_attn_W_router': _L0_attn_in['W_router'], 'L0_attn_G': _L0_attn_in['G'], 'L0_attn_W_up': _L0_attn_in['W_up'], 'L0_attn_ls2': _L0_attn_in['ls2'], 'L0_ffn_w1': _L0_ffn_in['w1'], 'L0_ffn_b1': _L0_ffn_in['b1'], 'L0_ffn_w2': _L0_ffn_in['w2'], 'L0_ffn_b2': _L0_ffn_in['b2'], 'L0_ffn_mfc1': _L0_ffn_in['mfc1'], 'L0_ffn_mact1': _L0_ffn_in['mact1'], 'L0_ffn_mact2': _L0_ffn_in['mact2'], 'L0_ffn_mfc2': _L0_ffn_in['mfc2'], 'L0_ffn_prelu_a': _L0_ffn_in['prelu_a']}

def reference(x, txt, L0_tok_channel_weights, L0_attn_rms1_w, L0_attn_W_in, L0_attn_dt_bias, L0_attn_W_out, L0_attn_ls1, L0_attn_rms2_w, L0_attn_W_down, L0_attn_W_router, L0_attn_G, L0_attn_W_up, L0_attn_ls2, L0_ffn_w1, L0_ffn_b1, L0_ffn_w2, L0_ffn_b2, L0_ffn_mfc1, L0_ffn_mact1, L0_ffn_mact2, L0_ffn_mfc2, L0_ffn_prelu_a):
    import jax
    import jax.numpy as jnp

    def _L0_tok_ref(x, channel_weights):
        import jax, jax.numpy as jnp
        import numpy as np
        IMG = 224
        PATCH = 16
        EMBED = 192
        C = 12
        B = 64
        Bb, Cc, H, W = x.shape
        K = PATCH
        n = H // K
        pooled = x.reshape(Bb, Cc, n, K, n, K).sum(axis=(3, 5))
        out = jnp.einsum('bcij,ce->bije', pooled, channel_weights)
        return out.reshape(Bb, n * n, EMBED)

    def _L0_attn_ref(x, rms1_w, W_in, dt_bias, W_out, ls1, rms2_w, W_down, W_router, G, W_up, ls2):
        import jax, jax.numpy as jnp
        import numpy as np
        D_MODEL = 192
        EXPAND = 4
        D_INNER = EXPAND * D_MODEL
        D_HEAD = 64
        N_HEADS = D_INNER // D_HEAD
        N_EXPERTS = 8
        TOP_K = 2
        R3 = 64
        R2 = 256
        EPS = 1e-05
        TANH_SCALE = 10.0
        ROUTER_TEMP = 0.5

        def _rms_norm(x, w):
            return x * jax.lax.rsqrt(jnp.mean(x * x, axis=-1, keepdims=True) + EPS) * w

        def _scaled_tanh(x):
            return TANH_SCALE * jnp.tanh(x * (1.0 / TANH_SCALE))
        B, L, _ = x.shape
        xn = _rms_norm(x, rms1_w)
        proj = xn @ W_in
        u, z, dt = jnp.split(proj, [D_INNER, 2 * D_INNER], axis=-1)
        log_alpha = -jax.nn.softplus(dt + dt_bias)
        alpha = jnp.exp(log_alpha)[..., None]
        u4 = u.reshape(B, L, N_HEADS, D_HEAD)

        def combine(left, right):
            a_l, b_l = left
            a_r, b_r = right
            return (a_r * a_l, a_r * b_l + b_r)
        _, h = jax.lax.associative_scan(combine, (jnp.broadcast_to(alpha, u4.shape), u4), axis=1)
        y = h.reshape(B, L, D_INNER) * jax.nn.silu(z)
        y = _scaled_tanh(y)
        x1 = x + ls1 * (y @ W_out)
        x2n = _rms_norm(x1, rms2_w)
        lat = _scaled_tanh(x2n @ W_down)
        logits = x2n @ W_router * (1.0 / ROUTER_TEMP)
        vals, idx = jax.lax.top_k(logits, TOP_K)
        probs = jax.nn.softmax(vals, axis=-1)
        w = jnp.sum(jax.nn.one_hot(idx, N_EXPERTS, dtype=lat.dtype) * probs[..., None], axis=-2)
        moe = jnp.einsum('blr,erc,ble->blc', lat, G, w)
        out = x1 + ls2 * (moe @ W_up)
        return out

    def _L0_ffn_ref(x, w1, b1, w2, b2, mfc1, mact1, mact2, mfc2, prelu_a):
        import jax, jax.numpy as jnp
        import numpy as np
        from jax import lax
        B, N, C, H = (64, 197, 192, 768)

        def quantize_linear(x, W, b):
            sf = lax.stop_gradient(jnp.mean(jnp.abs(W), axis=1, keepdims=True))
            rw = W - jnp.mean(W, axis=-1, keepdims=True)
            bw = sf * jnp.sign(rw)
            cw = jnp.clip(rw, -1.0, 1.0)
            weight = lax.stop_gradient(bw) - lax.stop_gradient(cw) + cw
            ci = jnp.clip(x, -1.0, 1.0)
            ba = lax.stop_gradient(jnp.sign(x)) - lax.stop_gradient(ci) + ci
            return jnp.einsum('bnc,hc->bnh', ba, weight) + b
        x = x + mfc1
        x = quantize_linear(x, w1, b1)
        x = x + mact1
        x = jnp.where(x >= 0, x, prelu_a * x)
        x = x + mact2
        x = x + mfc2
        x = quantize_linear(x, w2, b2)
        return x
    h = _L0_tok_ref(x, L0_tok_channel_weights)
    h = jnp.concatenate([h, txt], axis=1)
    h = h + _L0_attn_ref(_layernorm(h, axis=-1), L0_attn_rms1_w, L0_attn_W_in, L0_attn_dt_bias, L0_attn_W_out, L0_attn_ls1, L0_attn_rms2_w, L0_attn_W_down, L0_attn_W_router, L0_attn_G, L0_attn_W_up, L0_attn_ls2)
    h = h + _L0_ffn_ref(_layernorm(h, axis=-1), L0_ffn_w1, L0_ffn_b1, L0_ffn_w2, L0_ffn_b2, L0_ffn_mfc1, L0_ffn_mact1, L0_ffn_mact2, L0_ffn_mfc2, L0_ffn_prelu_a)
    return h

_drawn_inputs = setup_inputs


def setup_inputs(seed=0):
    import zlib

    import numpy as np

    out = dict(_drawn_inputs(seed))
    spreads = {'L0_attn_rms1_w': (1.0, 0.6),
     'L0_attn_ls1': (0.009999999776482582, 0.6),
     'L0_attn_rms2_w': (1.0, 0.6),
     'L0_attn_ls2': (0.009999999776482582, 0.6),
     'L0_ffn_b1': (0.0, 0.8),
     'L0_ffn_b2': (0.0, 2.0)}
    factors = {'L0_attn_W_in': 26.058,
     'L0_attn_dt_bias': 55.448,
     'L0_attn_W_out': 25.969,
     'L0_attn_W_down': 47.28,
     'L0_attn_W_router': 49.124,
     'L0_attn_G': 46.703,
     'L0_attn_W_up': 46.453,
     'L0_ffn_w1': 6.746,
     'L0_ffn_w2': 6.356}
    for name, (base, spread) in spreads.items():
        noise = np.random.default_rng([zlib.crc32(name.encode()), seed]).standard_normal(out[name].shape)
        drawn = base * np.exp(spread * noise) if base else spread * noise
        out[name] = jnp.asarray(drawn.astype(out[name].dtype))
    for name, factor in factors.items():
        out[name] = (out[name] * factor).astype(out[name].dtype)
    return out
```

```python
import concourse.bass as bass
from concourse import mybir
from contextlib import ExitStack


class Step:

    def __init__(self, eng, s, parity, groups):
        self.s, self.parity, self.groups, self.fixed = s, parity, groups, isinstance(s, int)
        self.eng, self.values = eng, {}

    def has(self, d):
        return not self.fixed or 0 <= self.s + d < self.groups

    def slot(self, d):
        return (self.parity + d) % 2

    def prepare(self, keys):
        if not self.fixed:
            for key in keys:
                self.count(*key)

    def reached(self, d):
        return not self.fixed or self.s + d >= 0

    def count(self, d, k=1, part=0):
        if self.fixed:
            if self.s + d >= self.groups:
                return self.groups * k
            return (self.s + d) * k + (part or k)
        if (d, k, part) not in self.values:
            self.values[d, k, part] = self.eng.snap((self.s + d) * k + (part or k))
        return self.values[d, k, part]


def fused_block(nc, x, txt, cw, rms1, w_in, dt_bias, w_out, ls1, rms2, w_down, w_router, g_exp, w_up, ls2,
                w1, b1, w2, b2, mfc1, mact1, mact2, mfc2, prelu_a, out):
    fp32, f32r, bf16, u32 = mybir.dt.float32, mybir.dt.float32r, mybir.dt.bfloat16, mybir.dt.uint32
    ALU, ACT, AX = mybir.AluOpType, mybir.ActivationFunctionType, mybir.AxisListType

    B, C, IMG, _ = x.shape
    TXT, D = txt.shape[1], txt.shape[2]
    K = 16
    NP_ = IMG // K
    IT = NP_ * NP_
    L = IT + TXT
    LP = L + 1
    GB = 2
    GROUPS = B // GB
    TT = 112
    NT = 5
    W = NT * TT
    WH = W // 2
    DI = w_out.shape[0]
    CT = DI // 128
    H = dt_bias.shape[0]
    HD = DI // H
    NE, R3, R2 = g_exp.shape
    ET = NE * R3 // 128
    NIN = 2 * DI + H
    D1 = D - 128
    FT = w1.shape[0] // 128
    SL = K * IMG
    EPS = 1e-5
    TS = 10.0
    XTILES = GB * C * NP_ // TT
    CH8 = TT // NP_

    row = nc.dram_tensor("row_scratch", (D,), fp32, kind="Internal").ap()
    scratch = nc.dram_tensor("alpha_scratch", (2, H, GB * LP), fp32, kind="Internal").ap()

    strips = x.rearrange("b c (i r) w -> (b c i) (r w)", r=K).rearrange("(g t p) n -> g t p n", t=XTILES, p=TT)

    ctx = ExitStack()
    with ctx:
        def sb(name, shape, dt=fp32):
            return ctx.enter_context(nc.sbuf_tensor(name, shape, dt))

        def sem(name):
            return ctx.enter_context(nc.semaphore(name))

        win_h = sb("win_h", [128, NIN], f32r)
        win_l = sb("win_l", [128, NIN], f32r)
        win_s = sb("win_s", [128, NIN], f32r)
        wout = sb("wout", [128, CT, D])
        ND = R3 + NE
        wd_h = sb("wd_h", [128, ND], f32r)
        wd_l = sb("wd_l", [128, ND], f32r)
        wd_s = sb("wd_s", [128, ND], f32r)
        gw = sb("gw", [128, ET, D])
        w1s = sb("w1s", [128, 2, DI], bf16)
        w2s = sb("w2s", [128, CT, D], bf16)
        cws = sb("cws", [C, D])
        sel = sb("sel", [2 * NE, ET * 128], f32r)
        ident = sb("ident", [128, 128])
        identb = sb("identb", [128, 128], bf16)
        nhalf = sb("nhalf", [TT, NT])
        epst = sb("epst", [TT, NT])
        invd = sb("invd", [TT, NT])
        mfc1c = sb("mfc1c", [TT, 1])
        iota = sb("iota", [TT, NE])
        hbias = sb("hbias", [H, 1])
        sf1 = sb("sf1", [128, CT])
        bias1 = sb("bias1", [128, CT])
        c2 = sb("c2", [128, 1])
        slope = sb("slope", [128, 1])
        side = sb("side", [128, 1])
        sf2r = sb("sf2r", [TT, D])
        b2r = sb("b2r", [TT, D])
        xs = sb("xs", [TT, XTILES, SL])
        pooled = [sb(f"pooled{i}", [TT, XTILES, NP_]) for i in range(2)]
        pT = sb("pT", [C, W])
        base = sb("base", [TT, NT, D])
        h0 = [sb(f"h0_{i}", [TT, NT, D]) for i in range(2)]
        xn0 = [sb(f"xn0_{i}", [TT, NT, D]) for i in range(2)]
        DX = 2 * 128
        xn = sb("xn", [TT, NT, DX])
        s01 = [sb(f"s01_{i}", [TT, NT, D]) for i in range(2)]
        h1 = sb("h1", [TT, NT, D])
        hb = sb("hb", [TT, NT, D])
        s8 = sb("s8", [TT, NT, D], bf16)
        ot = sb("ot", [TT, NT, D])
        st1 = sb("st1", [TT, NT, 6])
        mv1 = sb("mv1", [TT, NT, 2])
        st3 = sb("st3", [TT, NT, 6])
        mv3 = sb("mv3", [TT, NT, 2])
        sc1 = sb("sc1", [TT, 6, NT])
        sc2 = sb("sc2", [TT, 4, NT])
        sc3 = sb("sc3", [TT, 4, NT])
        ss = sb("ss", [TT, NT])
        lg = sb("lg", [TT, NT, NE])
        mx = sb("mx", [TT, NT, NE])
        ix = sb("ix", [TT, NT, NE], u32)
        ixf = sb("ixf", [TT, NT, 2])
        dd = sb("dd", [TT, NT])
        th = sb("th", [TT, NT])
        pp = sb("pp", [TT, 2, NT])
        e1 = sb("e1", [TT, NT, NE])
        e2 = sb("e2", [TT, NT, NE])
        wt = sb("wt", [TT, NT, NE])
        wc = sb("wc", [TT, NT, 2 * NE], f32r)
        xh = sb("xh", [128, 2, W], f32r)
        xl = sb("xl", [128, 2, W], f32r)
        x2h = sb("x2h", [128, 2, W], f32r)
        x2l = sb("x2l", [128, 2, W], f32r)
        al = sb("al", [H, GB * LP])
        alb = sb("alb", [128, 3, GB * LP])
        hs = [sb(f"hs{i}", [128, GB * LP]) for i in range(2)]
        sz = [sb(f"sz{i}", [128, GB * LP]) for i in range(2)]
        y = sb("y", [128, CT, W])
        lat = sb("lat", [128, W])
        lgT = sb("lgT", [ND, W])
        wT = sb("wT", [2 * NE, W], f32r)
        lw = sb("lw", [128, ET, W])
        sT = sb("sT", [128, 2, W], bf16)
        pre = [sb(f"pre{i}", [128, W]) for i in range(3)]
        q = sb("q", [128, FT, W], bf16)

        rc = sb("rc", [128, 4])
        nm1, nm2, sf2c = sb("nm1", [128, CT]), sb("nm2", [96, 2]), sb("sf2c", [96, 2])
        ma = sb("ma", [128, 3])

        ps = ctx.enter_context(nc.psum_tensor("ps", [128, 8, 512], fp32))
        U0, Z0, A0, B0 = 0, 2, 4, 6

        x_in = [sem(f"x_in{t}") for t in range(XTILES)]
        pool_done = [sem(f"pool_done{t}") for t in range(XTILES)]
        pT_in = sem("pT_in")
        txt_in = sem("txt_in")
        emb_done = sem("emb_done")
        h0_done = sem("h0_done")
        stat1, ag1 = sem("stat1"), sem("ag1")
        n1 = [sem(f"n1_{i}") for i in range(6)]
        r1_done = sem("r1_done")
        xn_part, xn_done = sem("xn_part"), sem("xn_done")
        xn0_done = sem("xn0_done")
        xT_done = sem("xT_done")
        xh_done, xl_done = sem("xh_done"), sem("xl_done")
        dt_done, dtt, al_done = sem("dt_done"), sem("dtt"), sem("al_done")
        al_out = sem("al_out")
        al_in = [sem(f"al_in{j}") for j in range(CT)]
        z_done = [sem(f"z_done{j}") for j in range(CT)]
        u_done = [[sem(f"u_done{j}_{b}") for b in range(GB)] for j in range(CT)]
        silu_done = [sem(f"silu_done{j}") for j in range(CT)]
        scan_done = [sem(f"scan_done{j}") for j in range(CT)]
        gate_done = [sem(f"gate_done{j}") for j in range(CT)]
        y_done = [sem(f"y_done{j}") for j in range(CT)]
        wo_done, x1_done = sem("wo_done"), sem("x1_done")
        s01_done = sem("s01_done")
        ss_done = sem("ss_done")
        n2 = [sem(f"n2_{i}") for i in range(2)]
        r2_done = sem("r2_done")
        x2_part, x2_done = sem("x2_part"), sem("x2_done")
        x2T_done, x2h_done, x2l_done = sem("x2T_done"), sem("x2h_done"), sem("x2l_done")
        lat_mm, lat_done = sem("lat_mm"), sem("lat_done")
        lat_dup = sem("lat_dup")
        lgT_done, lg_mm, lg_done = sem("lgT_done"), sem("lg_mm"), sem("lg_done")
        w_done, mx_done, ix_done = sem("w_done"), sem("mx_done"), sem("ix_done")
        th_done, pp_done = sem("th_done"), sem("pp_done")
        ee_done, e2_done, wsum_done = sem("ee_done"), sem("e2_done"), sem("wsum_done")
        wh_done, wc_done = sem("wh_done"), sem("wc_done")
        wT_mm, wT_done = sem("wT_mm"), sem("wT_done")
        wb_done = [sem(f"wb_done{k}") for k in range(ET)]
        lw_done = [sem(f"lw_done{k}") for k in range(ET)]
        g_done, h1_done = sem("g_done"), sem("h1_done")
        stat3, ag3 = sem("stat3"), sem("ag3")
        n3 = [sem(f"n3_{i}") for i in range(3)]
        r3_done, s8_done, hb_done = sem("r3_done"), sem("s8_done"), sem("hb_done")
        sT_mm, sT_done = sem("sT_mm"), sem("sT_done")
        f1_done = sem("f1_done")
        pre_done = sem("pre_done")
        leaky_done = sem("leaky_done")
        q_done = sem("q_done")
        f2_done, f2e_done, ot_done = sem("f2_done"), sem("f2e_done"), sem("ot_done")
        stored = sem("stored")
        win_dma, c_dma = sem("win_dma"), sem("c_dma")
        row_dma = sem("row_dma")
        set_p, set_v, set_a, set_w = sem("set_p"), sem("set_v"), sem("set_a"), sem("set_w")
        passed = sem("passed")

        yf = y[:, :, :].rearrange("p c n -> p (c n)")
        lwf = lw[:, :, :].rearrange("p c n -> p (c n)")
        raw_a, raw_b = yf[:, 0:NIN], yf[:, NIN:2 * NIN]
        raw_wo = lwf[:, 0:CT * D].rearrange("p (c n) -> p c n", c=CT)
        raw_g = lwf[:, CT * D:CT * D + ET * R2].rearrange("p (c n) -> p c n", c=ET)
        raw_up = hs[0][:, 0:2 * D].rearrange("p (c n) -> p c n", c=2)
        ls1b, ls2b = sz[0][:, 0:D], sz[0][:, D:2 * D]
        raw_d = [sz[1][:, i * (R3 + NE):(i + 1) * (R3 + NE)] for i in range(2)]
        scaled_d = [hs[1][:, i * ND:(i + 1) * ND] for i in range(2)]
        gT = [pre[i][:, 0:NE * R3] for i in range(2)]
        raw_w1 = alb[:, :, :].rearrange("p c n -> p (c n)")[:, 0:FT * D].rearrange("p (c n) -> p c n", c=FT)
        raw_w2 = [v[0:96, 0:4, :].rearrange("p t n -> p (t n)") for v in (s01[0], h1)]
        qf = q[:, :, :].rearrange("p c n -> p (c n)")
        sg1 = qf[:, 0:FT * D].rearrange("p (c n) -> p c n", c=FT)
        sg2 = qf[0:96, FT * D:FT * D + 2 * DI].rearrange("p (c n) -> p c n", c=2)

        spread = lat[0:NE, 0:ET * 128]

        def steps(eng, emit, needed):
            first, last = 4, GROUPS - 4
            for s in range(0, first):
                emit(Step(eng, s, s % 2, GROUPS))
            with eng.Fori(0, (last - first) // 2) as i:
                for u in range(2):
                    st = Step(eng, i * 2 + (first + u), (first + u) % 2, GROUPS)
                    st.prepare(needed)
                    emit(st)
            for s in range(last, GROUPS + 3):
                emit(Step(eng, s, s % 2, GROUPS))

        def five(bank):
            return ps[0:TT, bank:bank + 2, :].rearrange("p b n -> p (b n)")[:, 0:NT * D]

        def flat(buf):
            return buf[:, :, :].rearrange("p t n -> p (t n)")

        def tile_out(bank, t):
            a, b = t * D, (t + 1) * D
            if a < 512 < b:
                return [(slice(0, 512 - a), ps[0:TT, bank, a:512]), (slice(512 - a, D), ps[0:TT, bank + 1, 0:b - 512])]
            return [(slice(0, D), ps[0:TT, bank + a // 512, a % 512:a % 512 + D])]

        def signs_ps(bank):
            return ps[:, bank, :].bitcast(bf16)

        def f1_ps(st, j):
            if st.has(-1):
                p = A0 if j else B0
            else:
                p = (B0, A0)[j % 2]
            return ps[:, p:p + 2, 0:WH]

        cols2 = lambda v: v.rearrange("(a b) -> a b", b=1)
        weight_parts = [
            (raw_a, w_in[0:128, :]), (raw_b[0:D1, :], w_in[128:D, :]), (raw_b[64:64 + D1, :], w_in[128:D, :]),
            (rc[:, 0:1], cols2(rms1)[0:128, :]), (rc[0:D1, 1:2], cols2(rms1)[128:D, :]),
            (rc[64:64 + D1, 1:2], cols2(rms1)[128:D, :]),
            (rc[:, 2:3], cols2(rms2)[0:128, :]), (rc[0:D1, 3:4], cols2(rms2)[128:D, :]),
            (rc[64:64 + D1, 3:4], cols2(rms2)[128:D, :]),
            (hbias[:, :], cols2(dt_bias)), (cws[:, :], cw),
            (raw_wo, w_out.rearrange("(c p) n -> p c n", p=128)),
            (ls1b, ls1.partition_broadcast(128)), (ls2b, ls2.partition_broadcast(128)),
            (b2r[:, :], b2.partition_broadcast(TT)),
            (raw_d[0][:, 0:R3], w_down[0:128, :]), (raw_d[0][:, R3:R3 + NE], w_router[0:128, :]),
            (raw_d[1][0:D1, 0:R3], w_down[128:D, :]), (raw_d[1][64:128, 0:R3], w_down[128:D, :]),
            (raw_d[1][0:D1, R3:R3 + NE], w_router[128:D, :]), (raw_d[1][64:128, R3:R3 + NE], w_router[128:D, :]),
            (raw_g, g_exp.rearrange("e r c -> (e r) c").rearrange("(t p) c -> p t c", p=128)),
            (raw_up, w_up.rearrange("(k p) n -> p k n", p=128)),
            (raw_w1, w1.rearrange("(t p) n -> p t n", p=128)), (raw_w2[0], w2[0:96, :]), (raw_w2[1], w2[96:D, :]),
            (bias1[:, :], b1.rearrange("(t p) -> p t", p=128)),
            (ma[:, 0:1], mact1.rearrange("a b c -> (a b c)").partition_broadcast(128)),
            (ma[:, 1:2], mact2.rearrange("a b c -> (a b c)").partition_broadcast(128)),
            (ma[:, 2:3], mfc2.rearrange("a b c -> (a b c)").partition_broadcast(128)),
            (mfc1c[:, :], mfc1.rearrange("a b c -> (a b c)").partition_broadcast(TT)),
            (slope[:, :], prelu_a.partition_broadcast(128)),
        ]
        W_IN_PARTS = 6

        SET_ZEROS, SET_CONST, SET_SEL = 2, 9, 10
        SET_NM = SET_SF2 = 6
        SET_ALL = 14

        block = ctx.enter_context(nc.Block())

        @block.sync
        def _(sp):
            def store(st):
                b = (st.s - 4) * GB
                for dst, src in store_parts(b):
                    sp.dma_start(dst, src).then_inc(stored, 16)

            def decay_in(st, d, j):
                src = scratch[st.slot(d), 2 * j:2 * j + 2, :].unsqueeze(1).broadcast_to([2, HD, GB * LP])
                sp.dma_start(alb[:, j % 3, :], src).then_inc(al_in[j], 16)

            def step(st):
                s = st.s
                if st.has(0):
                    for j in range(3, CT):
                        sp.wait_ge(scan_done[j - 3], st.count(0))
                        decay_in(st, 0, j)
                if st.has(-4):
                    sp.wait_ge(ot_done, st.count(-4))
                    store(st)
                if st.has(3):
                    if st.reached(2):
                        sp.wait_ge(pool_done[1], st.count(2)).then_inc(passed, 1)
                    sp.dma_start(xs[:, 1, :], strips[s + 3, 1, :, :]).then_inc(x_in[1], 16)
                if st.has(2):
                    if st.reached(1):
                        sp.wait_ge(h0_done, st.count(1))
                    for dst, src in text_parts((s + 2) * GB):
                        sp.dma_start(dst, src).then_inc(txt_in, 16)
                if st.has(-1):
                    sp.wait_ge(lat_done, st.count(-1))
                    sp.dma_start(lat[R3:2 * R3, :], lat[0:R3, :]).then_inc(lat_dup, 16)
                if st.has(1):
                    sp.wait_ge(al_done, st.count(1))
                    sp.dma_start(scratch[st.slot(1)], al[:, :]).then_inc(al_out, 16)
                    sp.wait_ge(al_out, st.count(1, 16)).then_inc(passed, 1)
                    for j in range(3):
                        if st.reached(0):
                            sp.wait_ge(scan_done[j + 3], st.count(0))
                        decay_in(st, 1, j)
                if st.has(2):
                    for t in range(XTILES):
                        sp.wait_ge(pool_done[t], st.count(2)).then_inc(passed, 1)
                    if st.reached(1):
                        sp.wait_ge(emb_done, st.count(1))
                    half = TT // 2
                    for c0, p0, t, b in ((0, 0, 0, 0), (CH8, 0, 1, 0), (0, half, 1, 1), (4, 0, 2, 1)):
                        p1 = half if (t, b) == (1, 0) else TT
                        dst = pT[c0:c0 + (p1 - p0) // NP_, LP * b:LP * b + IT].rearrange("c (i j) -> c i j", j=NP_)
                        sp.dma_start(dst, pooled[st.slot(2)][p0:p1, t, :]).then_inc(pT_in, 16)
                if st.has(3):
                    for t in (0, 2):
                        sp.dma_start(xs[:, t, :], strips[s + 3, t, :, :]).then_inc(x_in[t], 16)

            def store_parts(b):
                o = out
                return [
                    (o[b, 0:2 * TT, :].rearrange("(t p) d -> p t d", p=TT), ot[:, 0:2, :]),
                    (o[b, 2 * TT:L, :], ot[0:L - 2 * TT, 2, :]),
                    (o[b + 1, 0:3 * TT - LP, :], ot[LP - 2 * TT:TT, 2, :]),
                    (o[b + 1, 3 * TT - LP:4 * TT - LP, :], ot[:, 3, :]),
                    (o[b + 1, 4 * TT - LP:L, :], ot[0:L + LP - 4 * TT, 4, :]),
                ]

            def text_parts(b):
                n = 2 * TT - IT
                return [
                    (base[TT - n:TT, 1, :], txt[b, 0:n, :]),
                    (base[0:TXT - n, 2, :], txt[b, n:TXT, :]),
                    (base[LP + IT - 4 * TT:LP + L - 4 * TT, 4, :], txt[b + 1, :, :]),
                ]

            for t in range(XTILES):
                sp.dma_start(xs[:, t, :], strips[0, t, :, :]).then_inc(x_in[t], 16)
            sp.wait_ge(set_p, SET_ZEROS)
            step(Step(sp, -2, 0, GROUPS))
            sp.wait_ge(set_v, SET_SF2)
            for c in range(2):
                part = row[c * 96:(c + 1) * 96].rearrange("(a b) -> a b", b=1)
                sp.dma_start(part, sf2c[:, c:c + 1]).then_inc(row_dma, 16)
            sp.wait_ge(row_dma, 32)
            sp.dma_start(sf2r[:, :], row.partition_broadcast(TT)).then_inc(row_dma, 16)
            sp.wait_ge(row_dma, 48)
            sp.wait_ge(set_p, SET_CONST)
            for k in range(2):
                sp.dma_start(sel[k * NE:(k + 1) * NE, :].bitcast(fp32), spread).then_inc(row_dma, 16)
            sp.wait_ge(set_a, 2)
            step(Step(sp, -1, 1, GROUPS))
            steps(sp, step, [(0, 1), (-1, 1), (-4, 1), (1, 1), (1, 16), (2, 1)])
            sp.wait_ge(ot_done, GROUPS)
            store(Step(sp, GROUPS + 3, 1, GROUPS))
            sp.wait_ge(stored, 80 * GROUPS)

        @block.gpsimd
        def _(pool):
            tt, ts = nc.gpsimd.tensor_tensor, nc.gpsimd.tensor_scalar

            nc.gpsimd.memset(base[:, :, :], 0.0).then_inc(set_p, 1)
            nc.gpsimd.memset(pT[:, :], 0.0).then_inc(set_p, 1)
            nc.gpsimd.memset(nhalf[:, :], -0.5)
            nc.gpsimd.memset(epst[:, :], EPS)
            nc.gpsimd.memset(invd[:, :], 1.0 / D)
            for e in range(NE):
                nc.gpsimd.memset(iota[:, e:e + 1], float(e))
            nc.gpsimd.memset(ident[:, :], 0.0).then_inc(set_p, 1)
            nc.gpsimd.memset(identb[:, :], 0.0).then_inc(set_p, 1)
            nc.gpsimd.memset(spread, 1.0).then_inc(set_p, 1)
            pool.wait_ge(set_p, 5)
            for m in (ident, identb):
                nc.gpsimd.affine_select(out=m[:, :], in_=m[:, :], compare_op=ALU.not_equal, fill=1.0, base=0,
                                        pattern=[[-1, 128]], channel_multiplier=1).then_inc(set_p, 1)
            nc.gpsimd.affine_select(out=spread, in_=spread, compare_op=ALU.is_ge, fill=0.0, base=0,
                                    pattern=[[1, ET * 128]], channel_multiplier=-R3).then_inc(set_p, 1)
            pool.wait_ge(set_p, 8)
            nc.gpsimd.affine_select(out=spread, in_=spread, compare_op=ALU.is_ge, fill=0.0, base=R3 - 1,
                                    pattern=[[-1, ET * 128]], channel_multiplier=R3).then_inc(set_p, 1)

            def step(st):
                if st.has(-3):
                    pool.wait_ge(ag3, st.count(-3))
                    if st.reached(-4):
                        pool.wait_ge(s8_done, st.count(-4))
                    tt(sc3[:, 0, :], mv3[:, :, 1], epst[:, :], ALU.add).then_inc(n3[0], 1)
                    pool.wait_ge(n3[0], st.count(-3))
                    tt(sc3[:, 1, :], sc3[:, 0, :], nhalf[:, :], ALU.pow).then_inc(n3[1], 1)
                    pool.wait_ge(n3[1], st.count(-3))
                    tt(sc3[:, 2, :], sc3[:, 1, :], mv3[:, :, 0], ALU.mult).then_inc(n3[2], 1)
                    pool.wait_ge(n3[2], st.count(-3))
                    tt(sc3[:, 3, :], mfc1c[:, :].broadcast_to([TT, NT]), sc3[:, 2, :], ALU.subtract).then_inc(r3_done, 1)
                    pool.wait_ge(h1_done, st.count(-3))
                    if st.reached(-4):
                        pool.wait_ge(ot_done, st.count(-4))
                    tt(hb[:, :, :], h1[:, :, :], b2r[:, :].unsqueeze(1).broadcast_to([TT, NT, D]),
                       ALU.add).then_inc(hb_done, 1)
                gate(st, 0)
                if st.has(-1):
                    pool.wait_ge(ss_done, st.count(-1))
                    if st.reached(-2):
                        pool.wait_ge(x2_done, st.count(-2))
                    tt(sc2[:, 0, :], ss[:, :], invd[:, :], ALU.mult).then_inc(n2[0], 1)
                    pool.wait_ge(n2[0], st.count(-1))
                    tt(sc2[:, 1, :], sc2[:, 0, :], epst[:, :], ALU.add).then_inc(n2[1], 1)
                    pool.wait_ge(n2[1], st.count(-1))
                    tt(sc2[:, 2, :], sc2[:, 1, :], nhalf[:, :], ALU.pow).then_inc(r2_done, 1)
                gate(st, 1)
                if st.has(-1):
                    pool.wait_ge(x1_done, st.count(-1))
                    if st.reached(-3):
                        pool.wait_ge(h1_done, st.count(-3))
                    tt(s01[st.slot(-1)][:, :, :], h0[st.slot(-1)][:, :, :], xn0[st.slot(-1)][:, :, :],
                       ALU.add).then_inc(s01_done, 1)
                gate(st, 2)
                gate(st, 3)
                if st.has(1):
                    first_norm(st)
                gate(st, 4)
                gate(st, 5)
                if st.has(-3):
                    pool.wait_ge(hb_done, st.count(-3))
                    pool.wait_ge(f2e_done, st.count(-3))
                    tt(ot[:, :, :], ot[:, :, :], hb[:, :, :], ALU.add).then_inc(ot_done, 1)

            def gate(st, j):
                if st.has(0):
                    pool.wait_ge(silu_done[j], st.count(0))
                    pool.wait_ge(scan_done[j], st.count(0))
                    tt(hs[j % 2][:, :], hs[j % 2][:, :], sz[j % 2][:, :], ALU.mult).then_inc(gate_done[j], 1)

            def first_norm(st):
                pool.wait_ge(ag1, st.count(1))
                if st.reached(0):
                    pool.wait_ge(xn_done, st.count(0))
                tt(sc1[:, 0, :], mv1[:, :, 1], epst[:, :], ALU.add).then_inc(n1[0], 1)
                pool.wait_ge(n1[0], st.count(1))
                tt(sc1[:, 1, :], sc1[:, 0, :], nhalf[:, :], ALU.pow).then_inc(n1[1], 1)
                pool.wait_ge(n1[1], st.count(1))
                tt(sc1[:, 2, :], sc1[:, 1, :], sc1[:, 1, :], ALU.mult).then_inc(n1[2], 1)
                pool.wait_ge(n1[2], st.count(1))
                tt(sc1[:, 3, :], sc1[:, 2, :], mv1[:, :, 1], ALU.mult).then_inc(n1[3], 1)
                pool.wait_ge(n1[3], st.count(1))
                tt(sc1[:, 4, :], sc1[:, 3, :], epst[:, :], ALU.add).then_inc(n1[4], 1)
                pool.wait_ge(n1[4], st.count(1))
                tt(sc1[:, 5, :], sc1[:, 4, :], nhalf[:, :], ALU.pow).then_inc(n1[5], 1)
                pool.wait_ge(n1[5], st.count(1))
                tt(sc1[:, 0, :], sc1[:, 5, :], sc1[:, 1, :], ALU.mult).then_inc(r1_done, 1)

            pool.wait_ge(c_dma, 16 * (len(weight_parts) - W_IN_PARTS))
            step(Step(pool, -1, 1, GROUPS))
            steps(pool, step, [(1, 1), (0, 1), (-1, 1), (-2, 1), (-3, 1), (-4, 1)])

        @block.scalar
        def _(act):
            act.preload_act_table_set("silu_and_others")
            a = nc.scalar.activation

            def hi(dst, bank):
                a(dst[:, :, 0:4 * TT], ps[:, bank:bank + 2, 0:4 * TT], ACT.Copy)
                return a(dst[:, :, 4 * TT:W], ps[:, bank + 2, 0:2 * TT].rearrange("p (c n) -> p c n", c=2), ACT.Copy)

            def tanh_gate(st, j):
                if st.has(0):
                    act.wait_ge(gate_done[j], st.count(0))
                    if j == 0:
                        if st.reached(-1):
                            act.wait_ge(wo_done, st.count(-1))
                    a(y[:, j, 0:GB * LP], hs[j % 2][:, :], ACT.Tanh, scale=1.0 / TS).then_inc(y_done[j], 1)

            def pool_part(st, t, j0, j1):
                if not st.has(2):
                    return
                if j0 == 0:
                    if st.reached(2):
                        act.wait_ge(x_in[t], st.count(2, 16))
                    if st.reached(0):
                        act.wait_ge(pT_in, st.count(0, 64))
                v = xs[:, t, :].rearrange("p (r j k) -> p j r k", r=K, j=NP_)
                for j in range(j0, j1):
                    i = a(v[:, j, :, :], v[:, j, :, :], ACT.Copy, accum_out=pooled[st.slot(2)][:, t, j:j + 1])
                if j1 == NP_:
                    i.then_inc(pool_done[t], 1)

            def silu(st, j):
                if st.has(0):
                    act.wait_ge(z_done[j], st.count(0))
                    if j >= 2:
                        act.wait_ge(gate_done[j - 2], st.count(0))
                    else:
                        if st.reached(-1):
                            act.wait_ge(gate_done[j + 4], st.count(-1))
                    a(sz[j % 2][:, :].rearrange("p (b n) -> p b n", b=GB), ps[:, Z0:Z0 + 2, 0:LP],
                      ACT.Silu).then_inc(silu_done[j], 1)

            def hidden(st, j):
                if st.has(-3):
                    act.wait_ge(f1_done, st.count(-3, FT, j + 1))
                    if j >= 3:
                        act.wait_ge(q_done, st.count(-3, FT, j - 2))
                    else:
                        if st.reached(-4):
                            act.wait_ge(q_done, st.count(-4, FT, j + 4))
                    a(pre[j % 3][:, :].rearrange("p (b n) -> p b n", b=2), f1_ps(st, j), ACT.Identity,
                      scale=sf1[:, j:j + 1], bias=bias1[:, j:j + 1]).then_inc(pre_done, 1)

            def hidden_sign(st, j):
                if st.has(-3):
                    act.wait_ge(leaky_done, st.count(-3, FT, j + 1))
                    if j == 0:
                        if st.reached(-4):
                            act.wait_ge(f2_done, st.count(-4))
                    a(q[:, j, :], pre[j % 3][:, :], ACT.Sign, scale=side[:, 0:1], bias=c2[:, 0:1]).then_inc(q_done, 1)

            def step(st):
                if st.has(-2):
                    act.wait_ge(mx_done, st.count(-2))
                    if st.reached(-3):
                        act.wait_ge(pp_done, st.count(-3))
                    a(th[:, :], dd[:, :], ACT.Tanh, scale=0.5).then_inc(th_done, 1)
                pool_part(st, 1, 0, 2)
                pool_part(st, 1, 2, 4)
                pool_part(st, 1, 4, 6)
                silu(st, 0)
                pool_part(st, 1, 6, 8)
                pool_part(st, 1, 8, 10)
                pool_part(st, 1, 10, 12)
                if st.has(-2):
                    act.wait_ge(wT_mm, st.count(-2))
                    if st.reached(-3):
                        act.wait_ge(wb_done[ET - 1], st.count(-3))
                    a(wT[:, 0:4 * TT], ps[0:2 * NE, B0, 0:4 * TT], ACT.Copy)
                    a(wT[:, 4 * TT:W], ps[0:2 * NE, B0 + 1, 0:TT], ACT.Copy).then_inc(wT_done, 1)
                if st.has(-3):
                    act.wait_ge(r3_done, st.count(-3))
                    if st.reached(-4):
                        act.wait_ge(sT_mm, st.count(-4))
                    for t in range(NT):
                        i = a(s8[:, t, :], h1[:, t, :], ACT.Sign, scale=sc3[:, 1, t:t + 1], bias=sc3[:, 3, t:t + 1])
                    i.then_inc(s8_done, 1)
                pool_part(st, 1, 12, NP_)
                silu(st, 1)
                tanh_gate(st, 0)
                if st.has(-3):
                    act.wait_ge(sT_mm, st.count(-3))
                    if st.reached(-4):
                        act.wait_ge(f1_done, st.count(-4, FT, FT))
                    a(sT[:, 0, :], signs_ps(A0)[:, 0:W], ACT.Copy)
                    a(sT[0:D1, 1, :], signs_ps(A0 + 1)[0:D1, 0:W], ACT.Copy).then_inc(sT_done, 1)
                silu(st, 2)
                pool_part(st, 2, 0, 2)
                tanh_gate(st, 1)
                hidden(st, 0)
                hidden(st, 1)
                silu(st, 3)
                pool_part(st, 2, 2, 4)
                hidden_sign(st, 0)
                tanh_gate(st, 2)
                hidden(st, 2)
                hidden_sign(st, 1)
                silu(st, 4)
                if st.has(-1):
                    act.wait_ge(x2T_done, st.count(-1))
                    if st.reached(-2):
                        act.wait_ge(lat_mm, st.count(-2))
                    hi(x2h, A0).then_inc(x2h_done, 1)
                hidden_sign(st, 2)
                silu(st, 5)
                tanh_gate(st, 3)
                hidden(st, 3)
                if st.has(-1):
                    act.wait_ge(lat_mm, st.count(-1))
                    if st.reached(-2):
                        act.wait_ge(lw_done[ET - 1], st.count(-2))
                    a(lat[0:R3, :].rearrange("p (b n) -> p b n", b=2), ps[0:R3, B0:B0 + 2, 0:WH], ACT.Tanh,
                      scale=1.0 / TS).then_inc(lat_done, 1)
                hidden(st, 4)
                tanh_gate(st, 4)
                hidden_sign(st, 3)
                hidden(st, 5)
                hidden_sign(st, 4)
                pool_part(st, 2, 4, 6)
                if st.has(1):
                    act.wait_ge(xT_done, st.count(1))
                    hi(xh, A0).then_inc(xh_done, 1)
                hidden_sign(st, 5)
                tanh_gate(st, 5)
                pool_part(st, 2, 6, 8)
                if st.has(1):
                    act.wait_ge(dt_done, st.count(1))
                    if st.reached(0):
                        act.wait_ge(al_out, st.count(0, 16))
                    a(al[:, :].rearrange("h (b n) -> h b n", b=GB), ps[0:H, Z0:Z0 + 2, 0:LP], ACT.Tanh, scale=0.5,
                      bias=hbias[:, 0:1]).then_inc(dtt, 1)
                    act.wait_ge(dtt, st.count(1))
                    a(al[:, :], al[:, :], ACT.Copy, scale=-0.5, bias=0.5).then_inc(al_done, 1)
                pool_part(st, 2, 8, 10)
                pool_part(st, 2, 10, 12)
                pool_part(st, 2, 12, NP_)

            for n, (dst, src) in enumerate(weight_parts):
                landed = win_dma if n < W_IN_PARTS else c_dma
                act.dma_start(dst, src, allow_slow_non_contiguous=True).then_inc(landed, 16)
            step(Step(act, -2, 0, GROUPS))
            act.wait_ge(c_dma, 16 * (len(weight_parts) - W_IN_PARTS))
            act.wait_ge(set_v, SET_NM)
            for t in range(CT):
                a(sg1[:, t, :], raw_w1[:, t, :], ACT.Sign, bias=nm1[:, t:t + 1])
            for t in range(2):
                a(sg2[:, t, :], raw_w2[t], ACT.Sign, bias=nm2[:, t:t + 1]).then_inc(set_a, 1)

            step(Step(act, -1, 1, GROUPS))
            act.wait_ge(set_v, SET_ALL)
            steps(act, step, [(2, 1), (2, 16), (1, 1), (0, 64), (0, 1), (0, 16), (-1, 1), (-2, 1), (-3, 1), (-4, 1)])

        @block.vector
        def _(dve):
            tt, ts, stt, cp = (nc.vector.tensor_tensor, nc.vector.tensor_scalar, nc.vector.scalar_tensor_tensor,
                               nc.vector.tensor_copy)
            n = [0]

            def then(i):
                n[0] += 1
                i.then_inc(set_v, 1)
                dve.wait_ge(set_v, n[0])

            def lo(dst, high, bank):
                tt(dst[:, :, 0:4 * TT], ps[:, bank:bank + 2, 0:4 * TT], high[:, :, 0:4 * TT].bitcast(fp32), ALU.subtract)
                return tt(dst[:, :, 4 * TT:W], ps[:, bank + 2, 0:2 * TT].rearrange("p (c n) -> p c n", c=2),
                          high[:, :, 4 * TT:W].bitcast(fp32), ALU.subtract)

            def pool_part(st, k):
                if st.has(2):
                    if k == 0:
                        dve.wait_ge(x_in[0], st.count(2, 16))
                        if st.reached(0):
                            dve.wait_ge(pT_in, st.count(0, 64))
                    v = xs[:, 0, :].rearrange("p (r j k) -> p j r k", r=K, j=NP_)
                    i = nc.vector.tensor_reduce(pooled[st.slot(2)][:, 0, 2 * k:2 * k + 2], v[:, 2 * k:2 * k + 2],
                                                AX.XY, ALU.add)
                    if k == NP_ // 2 - 1:
                        i.then_inc(pool_done[0], 1)

            def scan(st, j):
                if st.has(0):
                    dve.wait_ge(al_in[j], st.count(0, 16))
                    if j < 2:
                        if st.reached(-1):
                            dve.wait_ge(y_done[j + 4], st.count(-1))
                    else:
                        dve.wait_ge(y_done[j - 2], st.count(0))
                    for b in range(GB):
                        dve.wait_ge(u_done[j][b], st.count(0))
                        i = nc.vector.tensor_tensor_scan(hs[j % 2][:, b * LP:(b + 1) * LP],
                                                         alb[:, j % 3, b * LP:(b + 1) * LP],
                                                         ps[:, U0 + b, 0:LP], 0.0, ALU.mult, ALU.add)
                    i.then_inc(scan_done[j], 1)

            def stats(src, dst_s, dst_m, st, d, sem_s, sem_a):
                for t in range(NT):
                    i = nc.vector.bn_stats(dst_s[:, t, :], src[:, t, :])
                i.then_inc(sem_s, 1)
                dve.wait_ge(sem_s, st.count(d)).then_inc(passed, 1)
                for t in range(NT):
                    i = nc.vector.bn_aggr(dst_m[:, t, :], dst_s[:, t, :])
                i.then_inc(sem_a, 1)

            def step(st):
                x1, h, xn0n = xn0[st.slot(-1)], h0[st.slot(1)], xn0[st.slot(1)]
                if st.has(-2):
                    dve.wait_ge(th_done, st.count(-2))
                    spread_weights(st)
                scan(st, 0)
                weigh(st, 0)
                weigh(st, 1)
                weigh(st, 2)
                if st.has(-1):
                    dve.wait_ge(wo_done, st.count(-1))
                    tt(flat(x1), five(A0), flat(x1), ALU.add).then_inc(x1_done, 1)
                if st.has(-1):
                    dve.wait_ge(x1_done, st.count(-1))
                    dve.wait_ge(xT_done, st.count(0))
                    if st.reached(-2):
                        dve.wait_ge(r2_done, st.count(-2))
                    for t in range(NT):
                        i = stt(xn[:, t, 0:D], x1[:, t, :], 1.0, x1[:, t, :], ALU.mult, ALU.mult, accum_out=ss[:, t:t + 1])
                    i.then_inc(ss_done, 1)
                weigh(st, 3)
                scan(st, 1)
                pool_part(st, 0)
                if st.has(-1):
                    dve.wait_ge(r2_done, st.count(-1))
                    for t in range(NT):
                        i = ts(xn[:, t, 0:D], x1[:, t, :], sc2[:, 2, t:t + 1], None, ALU.mult)
                    i.then_inc(x2_part, 1)
                    dve.wait_ge(x2_part, st.count(-1))
                    cp(xn[:, :, D:DX], xn[:, :, 128:D]).then_inc(x2_done, 1)
                pool_part(st, 1)
                leaky(st, 0)
                scan(st, 2)
                leaky(st, 1)
                if st.has(1):
                    dve.wait_ge(emb_done, st.count(1))
                    dve.wait_ge(txt_in, st.count(1, 48))
                    if st.reached(-1):
                        dve.wait_ge(s01_done, st.count(-1))
                    tt(flat(h), five(B0), flat(base), ALU.add).then_inc(h0_done, 1)
                scan(st, 3)
                if st.has(1):
                    dve.wait_ge(h0_done, st.count(1))
                    if st.reached(0):
                        dve.wait_ge(xn0_done, st.count(0))
                    stats(h, st1, mv1, st, 1, stat1, ag1)
                leaky(st, 2)
                pool_part(st, 2)
                if st.has(-1):
                    dve.wait_ge(x2h_done, st.count(-1))
                    lo(x2l, x2h, A0).then_inc(x2l_done, 1)
                scan(st, 4)
                pool_part(st, 3)
                if st.has(1):
                    dve.wait_ge(r1_done, st.count(1))
                    if st.reached(-1):
                        dve.wait_ge(x2T_done, st.count(-1))
                    if st.reached(-1):
                        dve.wait_ge(s01_done, st.count(-1))
                    for t in range(NT):
                        i = ts(xn[:, t, 0:D], h[:, t, :], mv1[:, t, 0:1], sc1[:, 0, t:t + 1], ALU.subtract, ALU.mult)
                    i.then_inc(xn_part, 1)
                    dve.wait_ge(xn_part, st.count(1))
                    cp(xn[:, :, D:DX], xn[:, :, 128:D]).then_inc(xn_done, 1)
                leaky(st, 3)
                scan(st, 5)
                if st.has(-1):
                    dve.wait_ge(lat_mm, st.count(-1))
                    cp(lgT[R3:ND, :].rearrange("p (b n) -> p b n", b=2), ps[R3:ND, B0:B0 + 2, 0:WH]).then_inc(lgT_done, 1)
                leaky(st, 4)
                leaky(st, 5)
                pool_part(st, 4)
                if st.has(1):
                    dve.wait_ge(xh_done, st.count(1))
                    lo(xl, xh, A0).then_inc(xl_done, 1)
                if st.has(1):
                    if st.reached(-1):
                        dve.wait_ge(s01_done, st.count(-1))
                    for t in range(NT):
                        i = ts(xn0n[:, t, :], h[:, t, :], mv1[:, t, 0:1], sc1[:, 1, t:t + 1], ALU.subtract, ALU.mult)
                    i.then_inc(xn0_done, 1)
                if st.has(-1):
                    top_two(st)
                pool_part(st, 5)
                pool_part(st, 6)
                if st.has(-3):
                    dve.wait_ge(f2_done, st.count(-3))
                    if st.reached(-4):
                        dve.wait_ge(stored, st.count(-4, 80))
                    tt(ot[:, :, :], five(A0).rearrange("p (t n) -> p t n", t=NT),
                       sf2r[:, :].unsqueeze(1).broadcast_to([TT, NT, D]), ALU.mult).then_inc(f2e_done, 1)
                if st.has(-2):
                    dve.wait_ge(g_done, st.count(-2))
                    dve.wait_ge(s01_done, st.count(-2))
                    if st.reached(-3):
                        dve.wait_ge(s8_done, st.count(-3))
                    if st.reached(-3):
                        dve.wait_ge(hb_done, st.count(-3))
                    tt(flat(h1), five(U0), flat(s01[st.slot(-2)]), ALU.add).then_inc(h1_done, 1)
                if st.has(-2):
                    dve.wait_ge(h1_done, st.count(-2))
                    if st.reached(-3):
                        dve.wait_ge(r3_done, st.count(-3))
                    stats(h1, st3, mv3, st, -2, stat3, ag3)

            def leaky(st, j):
                if st.has(-3):
                    dve.wait_ge(pre_done, st.count(-3, FT, j + 1))
                    p = pre[j % 3][:, :]
                    stt(p, p, slope[:, 0:1], p, ALU.mult, ALU.max).then_inc(leaky_done, 1)

            def weigh(st, k):
                if st.has(-2):
                    dve.wait_ge(wb_done[k], st.count(-2))
                    if k == 0:
                        dve.wait_ge(lat_dup, st.count(-2, 16))
                        if st.reached(-3):
                            dve.wait_ge(g_done, st.count(-3))
                    tt(lw[:, k, :].rearrange("p (b n) -> p b n", b=2), ps[:, B0:B0 + 2, 0:WH],
                       lat[:, :].rearrange("p (b n) -> p b n", b=2), ALU.mult).then_inc(lw_done[k], 1)

            def top_two(st):
                dve.wait_ge(lg_mm, st.count(-1))
                if st.reached(-2):
                    dve.wait_ge(ix_done, st.count(-2))
                cp(lg[:, :, :], ps[0:TT, B0 + 1, 0:NT * NE].rearrange("p (t e) -> p t e", t=NT)).then_inc(lg_done, 1)
                dve.wait_ge(lg_done, st.count(-1)).then_inc(passed, 1)
                for t in range(NT):
                    i = nc.vector.max(mx[:, t, :], lg[:, t, :])
                i.then_inc(w_done, 1)
                dve.wait_ge(w_done, st.count(-1))
                tt(dd[:, :], mx[:, :, 0], mx[:, :, 1], ALU.subtract).then_inc(mx_done, 1)
                for t in range(NT):
                    i = nc.vector.max_index(ix[:, t, :], mx[:, t, :], lg[:, t, :])
                i.then_inc(ix_done, 1)

            def spread_weights(st):
                dve.wait_ge(ix_done, st.count(-2))
                if st.reached(-3):
                    dve.wait_ge(wT_mm, st.count(-3))
                cp(ixf[:, :, :], ix[:, :, 0:2])
                ts(pp[:, 0, :], th[:, :], 0.5, 0.5, ALU.mult, ALU.add)
                ts(pp[:, 1, :], th[:, :], -0.5, 0.5, ALU.mult, ALU.add).then_inc(pp_done, 1)
                dve.wait_ge(pp_done, st.count(-2))
                it = iota[:, :].unsqueeze(1).broadcast_to([TT, NT, NE])
                bc = [TT, NT, NE]
                tt(e1[:, :, :], it, ixf[:, :, 0:1].broadcast_to(bc), ALU.is_equal)
                tt(e2[:, :, :], it, ixf[:, :, 1:2].broadcast_to(bc), ALU.is_equal).then_inc(ee_done, 1)
                dve.wait_ge(ee_done, st.count(-2))
                tt(e1[:, :, :], e1[:, :, :], pp[:, 0, :].unsqueeze(2).broadcast_to(bc), ALU.mult)
                tt(e2[:, :, :], e2[:, :, :], pp[:, 1, :].unsqueeze(2).broadcast_to(bc), ALU.mult).then_inc(e2_done, 1)
                dve.wait_ge(e2_done, st.count(-2))
                tt(wt[:, :, :], e1[:, :, :], e2[:, :, :], ALU.add).then_inc(wsum_done, 1)
                dve.wait_ge(wsum_done, st.count(-2))
                cp(wc[:, :, 0:NE], wt[:, :, :]).then_inc(wh_done, 1)
                dve.wait_ge(wh_done, st.count(-2))
                tt(wc[:, :, NE:2 * NE], wt[:, :, :], wc[:, :, 0:NE].bitcast(fp32), ALU.subtract).then_inc(wc_done, 1)

            dve.wait_ge(win_dma, 16 * W_IN_PARTS)
            ts(raw_a, raw_a, rc[:, 0:1], None, ALU.mult)
            then(ts(raw_b, raw_b, rc[:, 1:2], None, ALU.mult))
            cp(win_h[:, :], raw_a)
            then(cp(win_s[:, :], raw_b))
            tt(win_l[:, :], raw_a, win_h[:, :].bitcast(fp32), ALU.subtract)
            then(tt(win_s[64:128, :], raw_b[64:128, :], win_s[64:128, :].bitcast(fp32), ALU.subtract))
            step(Step(dve, -2, 0, GROUPS))
            dve.wait_ge(c_dma, 16 * (len(weight_parts) - W_IN_PARTS))
            then(nc.vector.tensor_reduce(nm1[:, :], raw_w1, AX.X, ALU.add))
            nc.vector.tensor_reduce(sf1[:, :], raw_w1, AX.X, ALU.add, apply_absolute_value=True)
            for t in range(2):
                nc.vector.tensor_reduce(nm2[:, t:t + 1], raw_w2[t], AX.X, ALU.add)
                i = nc.vector.tensor_reduce(sf2c[:, t:t + 1], raw_w2[t], AX.X, ALU.add, apply_absolute_value=True)
            then(i)
            ts(nm1[:, :], nm1[:, :], -1.0 / D, None, ALU.mult)
            ts(nm2[:, :], nm2[:, :], -1.0 / DI, None, ALU.mult)
            ts(sf1[:, :], sf1[:, :], 1.0 / D, None, ALU.mult)
            ts(bias1[:, :], bias1[:, :], ma[:, 0:1], None, ALU.add)
            tt(c2[:, :], ma[:, 1:2], ma[:, 2:3], ALU.add)
            ts(side[:, :], slope[:, :], 1.0, 2.0, ALU.is_le, ALU.mult)
            ts(hbias[:, :], hbias[:, :], 0.5, None, ALU.mult)
            then(ts(sf2c[:, :], sf2c[:, :], 1.0 / DI, None, ALU.mult))
            assert n[0] == SET_SF2
            then(ts(side[:, :], side[:, :], -1.0, None, ALU.add))
            ts(sf1[:, :], sf1[:, :], side[:, 0:1], None, ALU.mult)
            then(ts(bias1[:, :], bias1[:, :], side[:, 0:1], None, ALU.mult))
            step(Step(dve, -1, 1, GROUPS))
            for i in range(2):
                c = rc[:, 2 + i:3 + i]
                ts(scaled_d[i][:, 0:R3], raw_d[i][:, 0:R3], c, None, ALU.mult)
                k = ts(scaled_d[i][:, R3:ND], raw_d[i][:, R3:ND], c, 2.0, ALU.mult, ALU.mult)
            then(k)
            cp(wd_h[:, :], scaled_d[0])
            then(cp(wd_s[:, :], scaled_d[1]))
            tt(wd_l[:, :], scaled_d[0], wd_h[:, :].bitcast(fp32), ALU.subtract)
            tt(wd_s[64:128, :], scaled_d[1][64:128, :], wd_s[64:128, :].bitcast(fp32), ALU.subtract)
            then(stt(wout[:, :, :], raw_wo, TS, ls1b.unsqueeze(1).broadcast_to([128, CT, D]), ALU.mult, ALU.mult))
            then(nc.vector.memset(y[:, :, GB * LP:W], 0.0))
            dve.wait_ge(set_w, 1)
            cp(w1s[:, 0, :], signs_ps(0)[:, 0:DI])
            cp(w1s[0:D1, 1, :], signs_ps(1)[0:D1, 0:DI])
            for c in range(2):
                cp(w2s[:, :, c * 96:(c + 1) * 96], signs_ps(2 + c)[:, 0:CT * 96].rearrange("p (t n) -> p t n", t=CT))
            for k in range(2):
                g = cp(gT[k], ps[:, 4 + k, 0:NE * R3])
            then(g)
            dve.wait_ge(set_w, 2)
            for k in range(ET):
                g = stt(gw[:, k, :], ps[:, 6 + k // 2, (k % 2) * D:(k % 2 + 1) * D], TS, ls2b, ALU.mult, ALU.mult)
            then(g)
            assert n[0] == SET_ALL
            dve.wait_ge(row_dma, 48)
            steps(dve, step, [(2, 16), (1, 1), (1, 48), (0, 64), (0, 1), (0, 16), (-1, 1), (-2, 1), (-2, 16), (-3, 1), (-4, 80)])

        @block.tensor
        def _(pe):
            mm, tr = nc.tensor.matmul, nc.tensor.transpose

            def project(dst, m, hi, lo, w_h, w_l, w_s, cols):
                mm(dst, w_h[:, m], hi[:, 0, cols], start=True, stop=False)
                mm(dst, w_h[:, m], lo[:, 0, cols], start=False, stop=False)
                mm(dst, w_l[:, m], hi[:, 0, cols], start=False, stop=False)
                mm(dst, w_s[:, m], hi[:, 1, cols], start=False, stop=False)
                return mm(dst, w_s[0:D1, m], lo[0:D1, 1, cols], start=False, stop=True)

            def z_tile(st, j):
                if st.has(0):
                    if j == 0:
                        pe.wait_ge(dtt, st.count(0))
                    else:
                        pe.wait_ge(silu_done[j - 1], st.count(0))
                    for b in range(GB):
                        i = project(ps[:, Z0 + b, 0:LP], slice(DI + j * 128, DI + (j + 1) * 128), xh, xl, win_h, win_l,
                                    win_s, slice(b * LP, (b + 1) * LP))
                    i.then_inc(z_done[j], 1)

            def u_tile(st, j):
                if st.has(0):
                    if j == 0:
                        if st.reached(-3):
                            pe.wait_ge(h1_done, st.count(-3))
                    else:
                        pe.wait_ge(scan_done[j - 1], st.count(0))
                    for b in range(GB):
                        project(ps[:, U0 + b, 0:LP], slice(j * 128, (j + 1) * 128), xh, xl, win_h, win_l,
                                win_s, slice(b * LP, (b + 1) * LP)).then_inc(u_done[j][b], 1)

            def transposes(bank, src):
                for t in range(NT):
                    for c in range(2):
                        dst = (ps[:, bank + c, t * TT:(t + 1) * TT] if t < 4 else ps[:, bank + 2, c * TT:(c + 1) * TT])
                        i = tr(dst, src[:, t, c * 128:(c + 1) * 128], ident[0:TT, 0:TT])
                return i

            def out_proj(st, t):
                if st.has(-1):
                    if t == 0:
                        for j in range(CT):
                            pe.wait_ge(y_done[j], st.count(-1))
                        if st.reached(-4):
                            pe.wait_ge(f2e_done, st.count(-4))
                        pe.wait_ge(xl_done, st.count(0))
                    for ch, dst in tile_out(A0, t):
                        for j in range(CT):
                            i = mm(dst, y[:, j, t * TT:(t + 1) * TT], wout[:, j, ch], start=j == 0, stop=j == CT - 1)
                    if t == NT - 1:
                        i.then_inc(wo_done, 1)

            def weight_rows(st):
                if st.has(-2):
                    pe.wait_ge(wc_done, st.count(-2))
                    pe.wait_ge(xl_done, st.count(0))
                    for t in range(NT):
                        dst = ps[0:2 * NE, B0, t * TT:(t + 1) * TT] if t < 4 else ps[0:2 * NE, B0 + 1, 0:TT]
                        i = tr(dst, wc[:, t, :].bitcast(fp32), ident[0:TT, 0:TT])
                    i.then_inc(wT_mm, 1)

            def spread_pair(st, k):
                if st.has(-2):
                    if k == 0:
                        pe.wait_ge(wT_done, st.count(-2))
                    else:
                        pe.wait_ge(lw_done[k - 1], st.count(-2))
                    for b in range(2):
                        i = mm(ps[:, B0 + b, 0:WH], sel[:, k * 128:(k + 1) * 128], wT[:, b * WH:(b + 1) * WH],
                               start=True, stop=True)
                    i.then_inc(wb_done[k], 1)

            def hidden(st, j):
                if st.has(-3):
                    if j == 0:
                        pe.wait_ge(sT_done, st.count(-3))
                        pe.wait_ge(lw_done[ET - 1], st.count(-2))
                        if st.reached(-4):
                            pe.wait_ge(pre_done, st.count(-4, FT, FT))
                    elif j >= 2:
                        read = j if st.has(-1) else j - 1
                        pe.wait_ge(pre_done, st.count(-3, FT, read))
                    if j == 3:
                        pe.wait_ge(x2l_done, st.count(-1))
                    for b in range(2):
                        cols = slice(b * WH, (b + 1) * WH)
                        mm(f1_ps(st, j)[:, b, :], w1s[:, 0, j * 128:(j + 1) * 128], sT[:, 0, cols], start=True, stop=False)
                        i = mm(f1_ps(st, j)[:, b, :], w1s[0:D1, 1, j * 128:(j + 1) * 128], sT[0:D1, 1, cols],
                               start=False, stop=True)
                    i.then_inc(f1_done, 1)

            def mixture(st, t):
                if st.has(-2):
                    if t == 0:
                        pe.wait_ge(lw_done[ET - 1], st.count(-2))
                        pe.wait_ge(scan_done[CT - 1], st.count(0))
                        if st.reached(-3):
                            pe.wait_ge(h1_done, st.count(-3))
                    for ch, dst in tile_out(U0, t):
                        for k in range(ET):
                            i = mm(dst, lw[:, k, t * TT:(t + 1) * TT], gw[:, k, ch], start=k == 0, stop=k == ET - 1)
                    if t == NT - 1:
                        i.then_inc(g_done, 1)

            def step(st):
                z_tile(st, 0)
                out_proj(st, 0)
                u_tile(st, 0)
                out_proj(st, 1)
                weight_rows(st)
                out_proj(st, 2)
                spread_pair(st, 0)
                out_proj(st, 3)
                spread_pair(st, 1)
                out_proj(st, 4)
                spread_pair(st, 2)
                z_tile(st, 1)
                spread_pair(st, 3)
                u_tile(st, 1)
                if st.has(-3):
                    pe.wait_ge(s8_done, st.count(-3))
                    pe.wait_ge(x1_done, st.count(-1))
                    if st.reached(-4):
                        pe.wait_ge(f2e_done, st.count(-4))
                    for t in range(NT):
                        tr(signs_ps(A0)[:, t * TT:(t + 1) * TT], s8[:, t, 0:128], identb[0:TT, 0:TT])
                        i = tr(signs_ps(A0 + 1)[0:D1, t * TT:(t + 1) * TT], s8[:, t, 128:D], identb[0:TT, 0:TT])
                    i.then_inc(sT_mm, 1)
                z_tile(st, 2)
                hidden(st, 0)
                u_tile(st, 2)
                hidden(st, 1)
                z_tile(st, 3)
                if st.has(1):
                    pe.wait_ge(pT_in, st.count(1, 64))
                    if st.reached(-3):
                        pe.wait_ge(pre_done, st.count(-3, FT, 1))
                    if st.reached(0):
                        pe.wait_ge(xl_done, st.count(0))
                    if not st.has(-3):
                        if st.reached(-2):
                            pe.wait_ge(lw_done[ET - 1], st.count(-2))
                    for t in range(NT):
                        for ch, dst in tile_out(B0, t):
                            i = mm(dst, pT[:, t * TT:(t + 1) * TT], cws[:, ch], start=True, stop=True)
                    i.then_inc(emb_done, 1)
                u_tile(st, 3)
                hidden(st, 2)
                z_tile(st, 4)
                if st.has(-1):
                    pe.wait_ge(x2_done, st.count(-1))
                    if st.reached(-3):
                        pe.wait_ge(pre_done, st.count(-3, FT, 3))
                    pe.wait_ge(h0_done, st.count(1))
                    transposes(A0, xn).then_inc(x2T_done, 1)
                u_tile(st, 4)
                z_tile(st, 5)
                hidden(st, 3)
                if st.has(-1):
                    pe.wait_ge(x2l_done, st.count(-1))
                    for b in range(2):
                        i = project(ps[0:ND, B0 + b, 0:WH], slice(0, ND), x2h, x2l, wd_h, wd_l, wd_s,
                                    slice(b * WH, (b + 1) * WH))
                    i.then_inc(lat_mm, 1)
                hidden(st, 4)
                u_tile(st, 5)
                hidden(st, 5)
                mixture(st, 0)
                if st.has(1):
                    pe.wait_ge(xn_done, st.count(1))
                    if st.reached(-3):
                        pe.wait_ge(pre_done, st.count(-3, FT, FT))
                    if st.reached(-1):
                        pe.wait_ge(lat_done, st.count(-1))
                    if st.reached(-1):
                        pe.wait_ge(lgT_done, st.count(-1))
                    transposes(A0, xn).then_inc(xT_done, 1)
                if st.has(-1):
                    pe.wait_ge(lat_done, st.count(-1)).then_inc(passed, 1)
                    pe.wait_ge(lgT_done, st.count(-1)).then_inc(passed, 1)
                    for t in range(NT):
                        i = tr(ps[0:TT, B0 + 1, t * NE:(t + 1) * NE], lgT[R3:ND, t * TT:(t + 1) * TT],
                               ident[R3:ND, R3:ND])
                    i.then_inc(lg_mm, 1)
                mixture(st, 1)
                mixture(st, 2)
                if st.has(1):
                    pe.wait_ge(xh_done, st.count(1))
                    pe.wait_ge(xl_done, st.count(1))
                    if st.reached(0):
                        pe.wait_ge(silu_done[CT - 1], st.count(0))
                    for b in range(GB):
                        i = project(ps[0:H, Z0 + b, 0:LP], slice(2 * DI, NIN), xh, xl, win_h, win_l, win_s,
                                    slice(b * LP, (b + 1) * LP))
                    i.then_inc(dt_done, 1)
                if st.has(-3):
                    pe.wait_ge(q_done, st.count(-3, FT, FT))
                    pe.wait_ge(xl_done, st.count(1))
                    for t in range(NT):
                        for ch, dst in tile_out(A0, t):
                            for j in range(FT):
                                i = mm(dst, q[:, j, t * TT:(t + 1) * TT], w2s[:, j, ch], start=j == 0, stop=j == FT - 1)
                    i.then_inc(f2_done, 1)
                mixture(st, 3)
                mixture(st, 4)

            pe.wait_ge(set_p, SET_CONST)
            pe.wait_ge(set_v, SET_SF2)
            step(Step(pe, -1, 1, GROUPS))
            pe.wait_ge(set_a, 2)
            pe.wait_ge(xl_done, 1)
            pe.wait_ge(dtt, 1)
            for t in range(CT):
                tr(signs_ps(0)[:, t * 128:(t + 1) * 128], sg1[:, t, 0:128], identb[:, :])
                tr(signs_ps(1)[0:D1, t * 128:(t + 1) * 128], sg1[:, t, 128:D], identb[:, :])
                for c in range(2):
                    tr(signs_ps(2 + c)[:, t * 96:(t + 1) * 96], sg2[:, c, t * 128:(t + 1) * 128], identb[0:96, 0:96])
            for t in range(ET):
                for k in range(2):
                    i = tr(ps[:, 4 + k, t * 128:(t + 1) * 128], raw_g[:, t, k * 128:(k + 1) * 128], ident[:, :])
            i.then_inc(set_w, 1)
            pe.wait_ge(set_v, SET_ALL - 1)
            for t in range(ET):
                for k in range(2):
                    i = mm(ps[:, 6 + t // 2, (t % 2) * D:(t % 2 + 1) * D], gT[k][:, t * 128:(t + 1) * 128], raw_up[:, k, :],
                           start=k == 0, stop=k == 1)
            i.then_inc(set_w, 1)
            pe.wait_ge(set_v, SET_ALL)
            pe.wait_ge(row_dma, 80)
            steps(pe, step, [(1, 1), (1, 64), (0, 1), (-1, 1), (-2, 1), (-3, 1), (-4, 1)])


_INS = ['x', 'txt', 'L0_tok_channel_weights', 'L0_attn_rms1_w', 'L0_attn_W_in', 'L0_attn_dt_bias', 'L0_attn_W_out',
        'L0_attn_ls1', 'L0_attn_rms2_w', 'L0_attn_W_down', 'L0_attn_W_router', 'L0_attn_G', 'L0_attn_W_up',
        'L0_attn_ls2', 'L0_ffn_w1', 'L0_ffn_b1', 'L0_ffn_w2', 'L0_ffn_b2', 'L0_ffn_mfc1', 'L0_ffn_mact1',
        'L0_ffn_mact2', 'L0_ffn_mfc2', 'L0_ffn_prelu_a']
_OUTS = [((32, 273, 192), 'float32')]


def kernel(**inputs):
    import numpy as _np
    import concourse.bacc as _bacc
    from concourse import mybir as _mybir
    from concourse.bass_utils import run_bass_kernel_spmd as _run

    nc = _bacc.Bacc("TRN2", target_bir_lowering=False, num_devices=1)
    arrays, args = {}, []
    for name in _INS:
        a = _np.ascontiguousarray(inputs[name])
        arrays[f"in_{name}_dram"] = a
        args.append(nc.dram_tensor(f"in_{name}_dram", a.shape, _mybir.dt.from_np(a.dtype), kind="ExternalInput").ap())
    for i, (shape, dtype) in enumerate(_OUTS):
        dt = _mybir.dt.from_np(_np.dtype(dtype))
        args.append(nc.dram_tensor(f"out_{i}_dram", shape, dt, kind="ExternalOutput").ap())
    fused_block(nc, *args)
    r = _run(nc, [arrays], core_ids=[0])
    got = tuple(r.results[0][f"out_{i}_dram"] for i in range(len(_OUTS)))
    return got[0]
```
